# Optimizing a Trainium2 kernel written in Bass

```python
import numpy as np
import jax
import jax.numpy as jnp

def _softmax(x, axis=-1):
    return jax.nn.softmax(x, axis=axis)

def _gelu(x):
    return jax.nn.gelu(x, approximate=True)

def _silu(x):
    return jax.nn.silu(x)

def _sigmoid(x):
    return jax.nn.sigmoid(x)

def _layernorm(x, axis=-1, eps=1e-05):
    m = jnp.mean(x, axis=axis, keepdims=True)
    v = jnp.var(x, axis=axis, keepdims=True)
    return (x - m) / jnp.sqrt(v + eps)

def _scatter_add(tgt, idx, src, axis=0):
    return tgt.at[idx].add(src)

def _segment_sum(src, seg, n):
    return jax.ops.segment_sum(src, seg, n)
kernel_name = 'mk_prb_d2_jaxref_r8_3a2b94'

def setup_inputs(seed: int=0):
    np.random.seed(seed)
    _w = jnp.asarray

    def _L0_attn_setup():
        import jax, jax.numpy as jnp
        import numpy as np
        import math
        DIM = 128
        D_STATE = 16
        D_CONV = 4
        EXPAND = 2
        D_INNER = EXPAND * DIM
        DT_RANK = math.ceil(DIM / 16)
        BATCH = 1
        SEQLEN = 256

        def _causal_depthwise_conv(x_bdl, conv_w, conv_b):
            y = jax.lax.conv_general_dilated(x_bdl, conv_w, window_strides=(1,), padding=[(D_CONV - 1, 0)], dimension_numbers=('NCH', 'OIH', 'NCH'), feature_group_count=D_INNER)
            return y + conv_b[None, :, None]

        def _mamba_forward(hidden_states, in_proj_w, conv_w, conv_b, x_proj_w, dt_proj_w, dt_bias, A_log, D_skip, out_proj_w):
            B_, L, _ = hidden_states.shape
            xz = jnp.einsum('bld,ed->ble', hidden_states, in_proj_w)
            x, z = jnp.split(xz, 2, axis=-1)
            x = _causal_depthwise_conv(x.transpose(0, 2, 1), conv_w, conv_b).transpose(0, 2, 1)
            u = jax.nn.silu(x)
            x_db = jnp.einsum('bld,ed->ble', u, x_proj_w)
            dt_r, Bm, Cm = jnp.split(x_db, [DT_RANK, DT_RANK + D_STATE], axis=-1)
            dt = jnp.einsum('blr,dr->bld', dt_r, dt_proj_w) + dt_bias
            delta = jax.nn.softplus(dt + dt_bias)
            A = -jnp.exp(A_log)

            def step(h, inp):
                dt_t, B_t, C_t, u_t = inp
                dA = jnp.exp(dt_t[:, :, None] * A)
                h = h * dA + (dt_t * u_t)[:, :, None] * B_t[:, None, :]
                y_t = jnp.einsum('bdn,bn->bd', h, C_t)
                return (h, y_t)
            h0 = jnp.zeros((B_, D_INNER, D_STATE), dtype=jnp.float32)
            xs = (delta.swapaxes(0, 1), Bm.swapaxes(0, 1), Cm.swapaxes(0, 1), u.swapaxes(0, 1))
            _, ys = jax.lax.scan(step, h0, xs)
            y = ys.swapaxes(0, 1) + u * D_skip
            y = y * jax.nn.silu(z)
            return jnp.einsum('bld,od->blo', y, out_proj_w)
        key = jax.random.key(seed)
        ks = jax.random.split(key, 8)
        hidden_states = jax.random.normal(ks[0], (BATCH, SEQLEN, DIM), dtype=jnp.float32)
        in_proj_w = jax.random.normal(ks[1], (2 * D_INNER, DIM), dtype=jnp.float32) * DIM ** (-0.5)
        conv_w = jax.random.normal(ks[2], (D_INNER, 1, D_CONV), dtype=jnp.float32) * D_CONV ** (-0.5)
        conv_b = jax.random.normal(ks[3], (D_INNER,), dtype=jnp.float32) * 0.01
        x_proj_w = jax.random.normal(ks[4], (DT_RANK + 2 * D_STATE, D_INNER), dtype=jnp.float32) * D_INNER ** (-0.5)
        dt_init_std = DT_RANK ** (-0.5)
        dt_proj_w = jax.random.uniform(ks[5], (D_INNER, DT_RANK), dtype=jnp.float32, minval=-dt_init_std, maxval=dt_init_std)
        dt = np.logspace(math.log10(0.001), math.log10(0.1), D_INNER).astype(np.float32)
        dt = np.maximum(dt, 0.0001)
        dt_bias = jnp.asarray(dt + np.log1p(-np.exp(-dt)), dtype=jnp.float32)
        A_log = jnp.tile(jnp.log(jnp.arange(1, D_STATE + 1, dtype=jnp.float32)), (D_INNER, 1))
        D_skip = jnp.ones((D_INNER,), dtype=jnp.float32)
        out_proj_w = jax.random.normal(ks[6], (DIM, D_INNER), dtype=jnp.float32) * D_INNER ** (-0.5)
        return {'hidden_states': hidden_states, 'in_proj_w': in_proj_w, 'conv_w': conv_w, 'conv_b': conv_b, 'x_proj_w': x_proj_w, 'dt_proj_w': dt_proj_w, 'dt_bias': dt_bias, 'A_log': A_log, 'D_skip': D_skip, 'out_proj_w': out_proj_w}
    _L0_attn_in = _L0_attn_setup()

    def _L0_ffn_setup():
        import jax, jax.numpy as jnp
        import numpy as np
        D_MODEL = 128
        H_SHARED = 256
        H_ROUTED = 128
        N_EXPERTS = 8
        TOP_K = 2
        key = jax.random.key(seed)
        ks = jax.random.split(key, 8)
        B, T = (2, 256)
        sc_d = 1.0 / np.sqrt(D_MODEL)
        sc_hs = 1.0 / np.sqrt(H_SHARED)
        sc_hr = 1.0 / np.sqrt(H_ROUTED)
        return {'x': jax.random.normal(ks[0], (B, T, D_MODEL), dtype=jnp.float32), 'router_w': jax.random.normal(ks[1], (N_EXPERTS, D_MODEL), dtype=jnp.float32) * sc_d, 'router_bias': jnp.zeros((N_EXPERTS,), dtype=jnp.float32), 'sw1': jax.random.normal(ks[2], (D_MODEL, H_SHARED), dtype=jnp.float32) * sc_d, 'sw3': jax.random.normal(ks[3], (D_MODEL, H_SHARED), dtype=jnp.float32) * sc_d, 'sw2': jax.random.normal(ks[4], (H_SHARED, D_MODEL), dtype=jnp.float32) * sc_hs, 'ew1': jax.random.normal(ks[5], (N_EXPERTS, D_MODEL, H_ROUTED), dtype=jnp.float32) * sc_d, 'ew2': jax.random.normal(ks[6], (N_EXPERTS, H_ROUTED, D_MODEL), dtype=jnp.float32) * sc_hr}
    _L0_ffn_in = _L0_ffn_setup()

    def _L1_attn_setup():
        import jax, jax.numpy as jnp
        import numpy as np
        from jax.scipy.special import logsumexp
        B, L, E = (2, 128, 128)
        H, D = (8, 64)
        N_ITERS = 20
        key = jax.random.key(seed)
        ks = jax.random.split(key, 5)
        s_in = 1.0 / np.sqrt(E)
        s_out = 1.0 / np.sqrt(H * D)
        return {'x': jax.random.normal(ks[0], (B, L, E), jnp.float32), 'Wq': jax.random.normal(ks[1], (E, H * D), jnp.float32) * s_in, 'bq': jnp.zeros((H * D,), jnp.float32), 'Wk': jax.random.normal(ks[2], (E, H * D), jnp.float32) * s_in, 'bk': jnp.zeros((H * D,), jnp.float32), 'Wv': jax.random.normal(ks[3], (E, H * D), jnp.float32) * s_in, 'bv': jnp.zeros((H * D,), jnp.float32), 'Wo': jax.random.normal(ks[4], (H * D, E), jnp.float32) * s_out, 'bo': jnp.zeros((E,), jnp.float32)}
    _L1_attn_in = _L1_attn_setup()

    def _L1_ffn_setup():
        import jax, jax.numpy as jnp
        import numpy as np
        EPS = 1e-06
        LN_EPS = 1e-05

        def _absmean_core(W):
            gamma = jnp.mean(jnp.abs(W)) + EPS
            Ws = W / gamma
            Wq = jnp.sign(Ws) * jnp.minimum(jnp.round(jnp.abs(Ws)), 1.0)
            return (Wq, gamma)

        @jax.custom_vjp
        def absmean(W):
            return _absmean_core(W)[0]

        def _absmean_fwd(W):
            Wq, gamma = _absmean_core(W)
            return (Wq, gamma)

        def _absmean_bwd(gamma, g):
            return (g / gamma,)
        absmean.defvjp(_absmean_fwd, _absmean_bwd)

        def layernorm(x, w, b, eps=LN_EPS):
            mu = jnp.mean(x, axis=-1, keepdims=True)
            var = jnp.mean((x - mu) ** 2, axis=-1, keepdims=True)
            return (x - mu) * jax.lax.rsqrt(var + eps) * w + b
        key = jax.random.key(seed)
        k1, k2, k3 = jax.random.split(key, 3)
        d, h = (128, 512)
        B, T = (8, 256)
        return {'x': jax.random.normal(k1, (B, T, d), jnp.float32), 'W_fc': jax.random.normal(k2, (h, d), jnp.float32), 'ln_w': jnp.ones((h,), jnp.float32), 'ln_b': jnp.zeros((h,), jnp.float32), 'W_proj': jax.random.normal(k3, (d, h), jnp.float32)}
    _L1_ffn_in = _L1_ffn_setup()
    _d = {'L0_attn_hidden_states': _L0_attn_in['hidden_states'], 'L0_attn_in_proj_w': _L0_attn_in['in_proj_w'], 'L0_attn_conv_w': _L0_attn_in['conv_w'], 'L0_attn_conv_b': _L0_attn_in['conv_b'], 'L0_attn_x_proj_w': _L0_attn_in['x_proj_w'], 'L0_attn_dt_proj_w': _L0_attn_in['dt_proj_w'], 'L0_attn_dt_bias': _L0_attn_in['dt_bias'], 'L0_attn_A_log': _L0_attn_in['A_log'], 'L0_attn_D_skip': _L0_attn_in['D_skip'], 'L0_attn_out_proj_w': _L0_attn_in['out_proj_w'], 'L0_ffn_router_w': _L0_ffn_in['router_w'], 'L0_ffn_router_bias': _L0_ffn_in['router_bias'], 'L0_ffn_sw1': _L0_ffn_in['sw1'], 'L0_ffn_sw3': _L0_ffn_in['sw3'], 'L0_ffn_sw2': _L0_ffn_in['sw2'], 'L0_ffn_ew1': _L0_ffn_in['ew1'], 'L0_ffn_ew2': _L0_ffn_in['ew2'], 'L1_attn_Wq': _L1_attn_in['Wq'], 'L1_attn_bq': _L1_attn_in['bq'], 'L1_attn_Wk': _L1_attn_in['Wk'], 'L1_attn_bk': _L1_attn_in['bk'], 'L1_attn_Wv': _L1_attn_in['Wv'], 'L1_attn_bv': _L1_attn_in['bv'], 'L1_attn_Wo': _L1_attn_in['Wo'], 'L1_attn_bo': _L1_attn_in['bo'], 'L1_ffn_W_fc': _L1_ffn_in['W_fc'], 'L1_ffn_ln_w': _L1_ffn_in['ln_w'], 'L1_ffn_ln_b': _L1_ffn_in['ln_b'], 'L1_ffn_W_proj': _L1_ffn_in['W_proj']}
    _x0 = _d['L0_attn_hidden_states']
    _d['L0_attn_hidden_states'] = jax.random.normal(jax.random.fold_in(jax.random.key(seed), 1), (2, 2048, 128), dtype=_x0.dtype)
    del _x0
    return _d

def reference(L0_attn_hidden_states, L0_attn_in_proj_w, L0_attn_conv_w, L0_attn_conv_b, L0_attn_x_proj_w, L0_attn_dt_proj_w, L0_attn_dt_bias, L0_attn_A_log, L0_attn_D_skip, L0_attn_out_proj_w, L0_ffn_router_w, L0_ffn_router_bias, L0_ffn_sw1, L0_ffn_sw3, L0_ffn_sw2, L0_ffn_ew1, L0_ffn_ew2, L1_attn_Wq, L1_attn_bq, L1_attn_Wk, L1_attn_bk, L1_attn_Wv, L1_attn_bv, L1_attn_Wo, L1_attn_bo, L1_ffn_W_fc, L1_ffn_ln_w, L1_ffn_ln_b, L1_ffn_W_proj):

    def _L0_attn_ref(hidden_states, in_proj_w, conv_w, conv_b, x_proj_w, dt_proj_w, dt_bias, A_log, D_skip, out_proj_w):
        import jax, jax.numpy as jnp
        import numpy as np
        import math
        DIM = 128
        D_STATE = 16
        D_CONV = 4
        EXPAND = 2
        D_INNER = EXPAND * DIM
        DT_RANK = math.ceil(DIM / 16)
        BATCH = 1
        SEQLEN = 256

        def _causal_depthwise_conv(x_bdl, conv_w, conv_b):
            y = jax.lax.conv_general_dilated(x_bdl, conv_w, window_strides=(1,), padding=[(D_CONV - 1, 0)], dimension_numbers=('NCH', 'OIH', 'NCH'), feature_group_count=D_INNER)
            return y + conv_b[None, :, None]

        def _mamba_forward(hidden_states, in_proj_w, conv_w, conv_b, x_proj_w, dt_proj_w, dt_bias, A_log, D_skip, out_proj_w):
            B_, L, _ = hidden_states.shape
            xz = jnp.einsum('bld,ed->ble', hidden_states, in_proj_w)
            x, z = jnp.split(xz, 2, axis=-1)
            x = _causal_depthwise_conv(x.transpose(0, 2, 1), conv_w, conv_b).transpose(0, 2, 1)
            u = jax.nn.silu(x)
            x_db = jnp.einsum('bld,ed->ble', u, x_proj_w)
            dt_r, Bm, Cm = jnp.split(x_db, [DT_RANK, DT_RANK + D_STATE], axis=-1)
            dt = jnp.einsum('blr,dr->bld', dt_r, dt_proj_w) + dt_bias
            delta = jax.nn.softplus(dt + dt_bias)
            A = -jnp.exp(A_log)

            def step(h, inp):
                dt_t, B_t, C_t, u_t = inp
                dA = jnp.exp(dt_t[:, :, None] * A)
                h = h * dA + (dt_t * u_t)[:, :, None] * B_t[:, None, :]
                y_t = jnp.einsum('bdn,bn->bd', h, C_t)
                return (h, y_t)
            h0 = jnp.zeros((B_, D_INNER, D_STATE), dtype=jnp.float32)
            xs = (delta.swapaxes(0, 1), Bm.swapaxes(0, 1), Cm.swapaxes(0, 1), u.swapaxes(0, 1))
            _, ys = jax.lax.scan(step, h0, xs)
            y = ys.swapaxes(0, 1) + u * D_skip
            y = y * jax.nn.silu(z)
            return jnp.einsum('bld,od->blo', y, out_proj_w)
        return _mamba_forward(hidden_states, in_proj_w, conv_w, conv_b, x_proj_w, dt_proj_w, dt_bias, A_log, D_skip, out_proj_w)

    def _L0_ffn_ref(x, router_w, router_bias, sw1, sw3, sw2, ew1, ew2):
        import jax, jax.numpy as jnp
        import numpy as np
        D_MODEL = 128
        H_SHARED = 256
        H_ROUTED = 128
        N_EXPERTS = 8
        TOP_K = 2
        B, T, C = x.shape
        xf = x.reshape(-1, C)
        shared_out = jax.nn.silu(xf @ sw1) * (xf @ sw3) @ sw2
        s = jax.nn.sigmoid((xf @ router_w.T).astype(jnp.float32))
        sel_scores = s + router_bias.astype(jnp.float32)
        _, topk_idx = jax.lax.top_k(sel_scores, TOP_K)
        s_sel = jnp.take_along_axis(s, topk_idx, axis=1)
        denom = s_sel.sum(axis=1, keepdims=True)
        gates = jnp.where(denom > 1e-09, s_sel / (denom + 1e-09), 1.0 / TOP_K).astype(x.dtype)
        one_hot = jax.nn.one_hot(topk_idx, N_EXPERTS, dtype=x.dtype)
        comb = jnp.einsum('nke,nk->ne', one_hot, gates)
        h = jax.nn.gelu(jnp.einsum('nd,edh->neh', xf, ew1), approximate=False)
        y = jnp.einsum('neh,ehd->ned', h, ew2)
        routed_out = jnp.einsum('ned,ne->nd', y, comb)
        return (shared_out + routed_out).reshape(B, T, C)

    def _L1_attn_ref(x, Wq, bq, Wk, bk, Wv, bv, Wo, bo):
        import jax, jax.numpy as jnp
        import numpy as np
        from jax.scipy.special import logsumexp
        B, L, E = (2, 128, 128)
        H, D = (8, 64)
        N_ITERS = 20
        b, l, e = x.shape

        def proj(W, bias):
            return (x @ W + bias).reshape(b, l, H, D).transpose(0, 2, 1, 3)
        q, k, v = (proj(Wq, bq), proj(Wk, bk), proj(Wv, bv))
        logits = jnp.einsum('bhqd,bhkd->bhqk', q, k) / jnp.sqrt(jnp.float32(D))

        def body(_, la):
            la = la - logsumexp(la, axis=-1, keepdims=True)
            la = la - logsumexp(la, axis=-2, keepdims=True)
            return la
        log_alpha = jax.lax.fori_loop(0, N_ITERS, body, logits)
        attn = jnp.exp(log_alpha)
        out = jnp.einsum('bhqk,bhkd->bhqd', attn, v)
        out = out.transpose(0, 2, 1, 3).reshape(b, l, H * D)
        return out @ Wo + bo

    def _L1_ffn_ref(x, W_fc, ln_w, ln_b, W_proj):
        import jax, jax.numpy as jnp
        import numpy as np
        EPS = 1e-06
        LN_EPS = 1e-05

        def _absmean_core(W):
            gamma = jnp.mean(jnp.abs(W)) + EPS
            Ws = W / gamma
            Wq = jnp.sign(Ws) * jnp.minimum(jnp.round(jnp.abs(Ws)), 1.0)
            return (Wq, gamma)

        @jax.custom_vjp
        def absmean(W):
            return _absmean_core(W)[0]

        def _absmean_fwd(W):
            Wq, gamma = _absmean_core(W)
            return (Wq, gamma)

        def _absmean_bwd(gamma, g):
            return (g / gamma,)
        absmean.defvjp(_absmean_fwd, _absmean_bwd)

        def layernorm(x, w, b, eps=LN_EPS):
            mu = jnp.mean(x, axis=-1, keepdims=True)
            var = jnp.mean((x - mu) ** 2, axis=-1, keepdims=True)
            return (x - mu) * jax.lax.rsqrt(var + eps) * w + b
        h = jnp.einsum('btd,hd->bth', x, absmean(W_fc))
        h = jax.nn.gelu(h, approximate=False)
        h = layernorm(h, ln_w, ln_b)
        return jnp.einsum('bth,dh->btd', h, absmean(W_proj))
    x = L0_attn_hidden_states
    xn = _layernorm(x, axis=-1)
    x = x + _L0_attn_ref(xn, L0_attn_in_proj_w, L0_attn_conv_w, L0_attn_conv_b, L0_attn_x_proj_w, L0_attn_dt_proj_w, L0_attn_dt_bias, L0_attn_A_log, L0_attn_D_skip, L0_attn_out_proj_w) + _L0_ffn_ref(xn, L0_ffn_router_w, L0_ffn_router_bias, L0_ffn_sw1, L0_ffn_sw3, L0_ffn_sw2, L0_ffn_ew1, L0_ffn_ew2)
    xn = _layernorm(x, axis=-1)
    x = x + _L1_attn_ref(xn, L1_attn_Wq, L1_attn_bq, L1_attn_Wk, L1_attn_bk, L1_attn_Wv, L1_attn_bv, L1_attn_Wo, L1_attn_bo) + _L1_ffn_ref(xn, L1_ffn_W_fc, L1_ffn_ln_w, L1_ffn_ln_b, L1_ffn_W_proj)
    return x

_drawn_inputs = setup_inputs


def setup_inputs(seed=0):
    import zlib

    import numpy as np

    out = dict(_drawn_inputs(seed))
    spreads = {'L0_attn_D_skip': (1.0, 0.2),
     'L0_ffn_router_bias': (0.0, 0.1),
     'L1_attn_bq': (0.0, 0.8),
     'L1_attn_bk': (0.0, 2.0),
     'L1_attn_bv': (0.0, 0.8),
     'L1_attn_bo': (0.0, 2.0),
     'L1_ffn_ln_w': (1.0, 0.2),
     'L1_ffn_ln_b': (0.0, 0.323)}
    factors = {'L0_attn_conv_b': 8.0,
     'L0_attn_x_proj_w': 3.691,
     'L0_attn_dt_proj_w': 8.0,
     'L0_attn_dt_bias': 4.078,
     'L0_attn_A_log': 4.891,
     'L1_attn_Wq': 8.0,
     'L1_attn_Wk': 8.0,
     'L1_attn_Wv': 7.481,
     'L1_attn_Wo': 5.989}
    for name, (base, spread) in spreads.items():
        noise = np.random.default_rng([zlib.crc32(name.encode()), seed]).standard_normal(out[name].shape)
        drawn = base * np.exp(spread * noise) if base else spread * noise
        out[name] = jnp.asarray(drawn.astype(out[name].dtype))
    for name, factor in factors.items():
        out[name] = (out[name] * factor).astype(out[name].dtype)
    return out
```

```python
from contextlib import ExitStack, nullcontext

import concourse.bass as bass
from concourse import mybir

F32 = mybir.dt.float32
I32 = mybir.dt.int32
ALU = mybir.AluOpType
ACT = mybir.ActivationFunctionType
AX = mybir.AxisListType

P = 128
CH = 512
SEQ = 2048
NT = SEQ // P
NC = SEQ // CH
BATCHES = 2
HEADS = 8
HD = 64
FEATURE_ROWS = [p for p in range(P) if p % 32][:HD]
ITERS = 20
FAST = ITERS - 1
REFRESH = 4
LIFT = 2.0 ** 64
LN_LIFT = 64 * 0.6931471805599453
FLOOR = 2.0 ** -80
SAFE_ROWSUM = 2.1e-4


def sinkhorn(nc, xn_T, Wq, bq, Wk, bk, Wv, bv, head_out, rowsum_floor, general, batches=BATCHES, heads=HEADS,
             verdict=None):
    steps = 2 * ITERS if general else 2
    with ExitStack() as ctx:
        def sb(name, shape, dt=F32):
            return ctx.enter_context(nc.sbuf_tensor(("g_" if general else "f_") + name, shape, dt))

        def sem(name):
            return ctx.enter_context(nc.semaphore(("g_" if general else "f_") + name))

        expo = sb("expo", [P, NT, SEQ])
        xT = sb("xT", [P, SEQ])
        qq = sb("qq", [P, SEQ])
        kk = sb("kk", [P, SEQ])
        vals = sb("vals", [P, NT, HD])
        wq = sb("wq", [P, P])
        wk = sb("wk", [P, P])
        wv = sb("wv", [P, HD])
        bq_col = sb("bq_col", [P, 1])
        bk_col = sb("bk_col", [P, 1])
        bv_row = sb("bv_row", [1, HD])
        bq_scaled = sb("bq_scaled", [P, 1])
        ones = sb("ones", [1, P])
        sel = sb("sel", [P, NC, P])
        ident = sb("ident", [P, P])
        crow = sb("crow", [P, CH])
        negmax = sb("negmax", [P, NT])
        expbias = sb("expbias", [P, NT])
        total = sb("total", [P, 2, NT])
        lntotal = sb("lntotal", [P, NT])
        negpot = sb("negpot", [P, NT])
        w = sb("w", [P, NT])
        wlift = sb("wlift", [P, NT])
        lnrow = sb("lnrow", [P, CH])
        qrow = sb("qrow", [P, CH])
        parts = sb("parts", [P, REFRESH, NC])
        outT = sb("outT", [P, 2, CH])
        least = sb("least", [P, 2])
        banks = ctx.enter_context(nc.psum_tensor("g_banks" if general else "f_banks", [P, 8, CH], F32))

        sp_steps = sem("sp_steps")
        weights_loaded = sem("weights_loaded")
        x_loaded = sem("x_loaded")
        const_ready = sem("const_ready")
        bias_scaled = sem("bias_scaled")
        q_made, k_made, v_made = sem("q_made"), sem("k_made"), sem("v_made")
        q_stored, k_stored, v_stored = sem("q_stored"), sem("k_stored"), sem("v_stored")
        logits_ready = sem("logits_ready")
        max_ready = sem("max_ready")
        bias_ready = sem("bias_ready")
        exp_done = sem("exp_done")
        lntotal_ready = sem("lntotal_ready")
        negpot_ready = sem("negpot_ready")
        row_made = sem("row_made")
        row_stored = sem("row_stored")
        w_ready = sem("w_ready")
        rowsum_ready = sem("rowsum_ready")
        lnrow_ready = sem("lnrow_ready")
        qrow_ready = sem("qrow_ready")
        qbroad_ready = sem("qbroad_ready")
        oldtotal_ready = sem("oldtotal_ready")
        floored = sem("floored")
        rrow_ready = sem("rrow_ready")
        expbias_ready = sem("expbias_ready")
        unit_ready = sem("unit_ready")
        unit_done = sem("unit_done")
        sum_done = sem("sum_done")
        least_ready = sem("least_ready")
        wlast_ready = sem("wlast_ready")
        v_scaled = sem("v_scaled")
        out_made = sem("out_made")
        out_stored = sem("out_stored")
        out_written = sem("out_written")
        floor_loaded = sem("floor_loaded")

        WLOADS = 6
        CONSTS = 4 + NC
        WPER = NT * ITERS if not general else NT

        def flat(tensor, first, count):
            return tensor[:, first:first + count, :].rearrange("p c n -> p (c n)")

        def refreshed(u):
            return [REFRESH * u + r for r in range(REFRESH)]

        def order(u):
            fresh = [(j, r) for r, j in enumerate(refreshed(u))]
            old = [(j, None) for j in range(NT) if j not in refreshed(u)]
            return old[0:3] + fresh[0:1] + old[3:5] + fresh[1:2] + old[5:7] + fresh[2:3] + old[7:9] + fresh[3:4] + old[9:12]

        def if_needed(eng):
            if verdict is None:
                return nullcontext()
            return eng.If(eng.value_load(verdict[0:1, 0:1], min_val=0, max_val=1) == 1)

        block = ctx.enter_context(nc.Block())

        def sync_program(sp):
            with sp.Fori(0, batches) as b:
                sp.dma_start(xT[:, :], xn_T[:, bass.ds(b * SEQ, SEQ)]).then_inc(x_loaded, 16)
                with sp.Fori(0, heads) as h:
                    n = b * heads + h
                    cols = bass.ds(h * HD, HD)
                    head_rows = bass.ds(h * P, P)
                    sp.dma_start(wq[:, :], Wq[:, head_rows]).then_inc(weights_loaded, 16)
                    sp.dma_start(wk[:, :], Wk[:, head_rows]).then_inc(weights_loaded, 16)
                    sp.dma_start(bq_col[:, :], bq[head_rows, :]).then_inc(weights_loaded, 16)
                    sp.dma_start(bk_col[:, :], bk[head_rows, :]).then_inc(weights_loaded, 16)
                    sp.dma_start(wv[:, :], Wv[:, cols]).then_inc(weights_loaded, 16)
                    sp.dma_start(bv_row[:, :], bv[:, cols]).then_inc(weights_loaded, 16)
                    sp.wait_ge(out_stored, n + 1)
                    sp.sem_inc(sp_steps, 1)
                    for half in range(2):
                        dst = head_out[bass.ds(n, 1), :, :].rearrange(
                            "o d (k a n) -> a (o d) k n", k=2, a=2)[half]
                        sp.dma_start(dst, outT[HD * half:HD * half + HD, :, :]).then_inc(out_written, 16)
                    sp.wait_ge(out_written, 32 * (n + 1))
                    sp.sem_inc(sp_steps, 1)
            if not general:
                sp.wait_ge(least_ready, 2 * batches * heads + 1)
                sp.dma_start(rowsum_floor, least[:, 0:1]).then_inc(floor_loaded, 16)
                sp.wait_ge(floor_loaded, 16)

        @block.sync
        def _(sp):
            with if_needed(sp):
                sync_program(sp)

        def tensor_program(pe):
            def project(b, n):
                pe.wait_ge(x_loaded, 16 * (b + 1))
                pe.wait_ge(weights_loaded, 16 * WLOADS * (n + 1))
                for c in range(NC):
                    last = pe.matmul(banks[:, c, :], wq[:, :], xT[:, c * CH:(c + 1) * CH], start=True, stop=True)
                last.then_inc(q_made, 1)
                for c in range(NC):
                    last = pe.matmul(banks[:, NC + c, :], wk[:, :], xT[:, c * CH:(c + 1) * CH], start=True, stop=True)
                last.then_inc(k_made, 1)
                pe.wait_ge(q_stored, n + 1)
                for t in range(NT):
                    out = banks[:, t // 8, (t % 8) * HD:(t % 8) * HD + HD]
                    pe.matmul(out, xT[:, t * P:(t + 1) * P], wv[:, :], start=True, stop=False)
                    last = pe.matmul(out, ones[0:1, :], bv_row[:, :], start=False, stop=True)
                last.then_inc(v_made, 1)

            def logits(n, g, columns):
                pe.wait_ge(v_stored, n + 1)
                pe.wait_ge(k_stored, n + 1)
                left, right = (kk, qq) if columns else (qq, kk)
                for t in range(NT):
                    if t >= 2:
                        pe.wait_ge(exp_done, NT * g + t - 1)
                    for c in range(NC):
                        bank = banks[:, NC * (t % 2) + c, :]
                        last = pe.matmul(bank, left[:, t * P:(t + 1) * P], right[:, c * CH:(c + 1) * CH],
                                         start=True, stop=columns or not general)
                        if general and not columns:
                            last = pe.matmul(bank, sel[:, c, :], crow[:, :], start=False, stop=True)
                    last.then_inc(logits_ready, 1)

            def turn_row(r):
                pe.wait_ge(negpot_ready, r + 1)
                for t in range(NT):
                    c, k = t // 4, t % 4
                    last = pe.matmul(banks[32 * c:32 * c + 1, 0, k * P:(k + 1) * P], negpot[:, t:t + 1],
                                     ident[:, :], start=True, stop=True)
                last.then_inc(row_made, 1)
                pe.wait_ge(row_stored, r + 1)

            def rowsum(j, first, last_one):
                for c in range(NC):
                    last = pe.matmul(banks[32 * c:32 * c + 1, 7, :], w[:, j:j + 1],
                                     expo[:, j, c * CH:(c + 1) * CH], start=first, stop=last_one)
                return last

            def fresh_logits(i, lu, j):
                c = lu % NC
                if lu < NC:
                    pe.wait_ge(rrow_ready, NC * i + c + 1)
                if lu >= 3:
                    pe.wait_ge(unit_done, NT * i + lu - 2)
                pe.matmul(banks[:, 4 + lu % 3, :], kk[:, j * P:(j + 1) * P], qq[:, c * CH:(c + 1) * CH],
                          start=True, stop=True).then_inc(unit_ready, 1)

            def iteration(i, wdone, u, last_iteration):
                pe.wait_ge(qrow_ready, i + 1)
                for c in range(NC):
                    last = pe.matmul(banks[:, c, :], sel[:, c, :], qrow[:, :], start=True, stop=True)
                last.then_inc(qbroad_ready, 1)
                tiles = refreshed(u)
                units = [(lu, tiles[lu // NC]) for lu in range(NC * REFRESH)]
                for lu, j in units[:NC]:
                    fresh_logits(i, lu, j)
                for k, (j, r) in enumerate(order(u)):
                    for lu, jj in units[NC + 2 * k:NC + 2 * k + 2]:
                        fresh_logits(i, lu, jj)
                    pe.wait_ge(w_ready, wdone + k + 1)
                    if not last_iteration:
                        last = rowsum(j, k == 0, k == NT - 1)
                if not last_iteration:
                    last.then_inc(rowsum_ready, 1)

            def values(n):
                pe.wait_ge(v_scaled, n + 1)
                fresh = list(range(NT)) if general else refreshed(FAST % 4 - 1)
                tiles = [t for t in range(NT) if t not in fresh] + fresh
                for k, t in enumerate(tiles):
                    if t in fresh:
                        pe.wait_ge(floored, len(fresh) * n + fresh.index(t) + 1)
                    for c in range(NC):
                        last = pe.matmul(banks[HD * (c % 2):HD * (c % 2) + HD, c // 2, :], vals[:, t, :],
                                         expo[:, t, c * CH:(c + 1) * CH], start=(k == 0), stop=(k == NT - 1))
                last.then_inc(out_made, 1)

            pe.wait_ge(const_ready, CONSTS)
            with pe.Fori(0, batches) as b:
                with pe.Fori(0, heads) as h:
                    n = b * heads + h
                    project(b, n)
                    if general:
                        with pe.Fori(0, ITERS) as it:
                            g = n * steps + 2 * it
                            logits(n, g, False)
                            turn_row(g)
                            logits(n, g + 1, True)
                            turn_row(g + 1)
                    else:
                        logits(n, 2 * n, False)
                        turn_row(n)
                        logits(n, 2 * n + 1, True)
                        pe.wait_ge(w_ready, WPER * n + NT)
                        for j in range(NT):
                            last = rowsum(j, j == 0, j == NT - 1)
                        last.then_inc(rowsum_ready, 1)
                        with pe.Fori(0, FAST // 4) as q:
                            for u in range(4):
                                iteration(n * FAST + q * 4 + u, n * WPER + q * (4 * NT) + (u + 1) * NT, u, False)
                        for u in range(FAST % 4):
                            done = FAST // 4 * 4 + u
                            iteration(n * FAST + done, n * WPER + (done + 1) * NT, u, u == FAST % 4 - 1)
                    values(n)

        @block.tensor
        def _(pe):
            with if_needed(pe):
                tensor_program(pe)

        def scalar_program(act):
            def project(n):
                act.wait_ge(bias_scaled, n + 1)
                act.wait_ge(q_made, n + 1)
                act.activation(qq[:, :], flat(banks, 0, NC), ACT.Identity, bias=bq_scaled[:, :],
                               scale=HD ** -0.5).then_inc(q_stored, 1)
                act.wait_ge(v_made, n + 1)
                act.activation(vals[:, :, :].rearrange("p t d -> p (t d)"), flat(banks, 0, 2),
                               ACT.Copy).then_inc(v_stored, 1)

            def exponentials(g):
                for t in range(NT):
                    act.wait_ge(bias_ready, NT * g + t + 1)
                    act.activation(expo[:, t, :], flat(banks, NC * (t % 2), NC), ACT.Exp,
                                   bias=expbias[:, t:t + 1], accum_out=total[:, 1, t:t + 1]).then_inc(exp_done, 1)

            def log_totals(g):
                act.wait_ge(exp_done, NT * g + NT)
                act.activation(lntotal[:, :], total[:, 1, :], ACT.Ln, scale=1.0 / LIFT).then_inc(lntotal_ready, 1)

            def iteration(i, u):
                act.wait_ge(rowsum_ready, i + 1)
                act.activation(lnrow[:, :], banks[:, 7, :], ACT.Ln).then_inc(lnrow_ready, 1)
                act.wait_ge(lnrow_ready, i + 1)
                act.activation(qrow[:, :], lnrow[:, :], ACT.Exp, scale=-1.0).then_inc(qrow_ready, 1)
                group = slice(REFRESH * u, REFRESH * (u + 1))
                act.activation(lntotal[:, group], total[:, (u + 1) % 2, group], ACT.Ln,
                               scale=1.0 / LIFT).then_inc(oldtotal_ready, 1)
                act.wait_ge(expbias_ready, i + 1)
                for lu in range(NC * REFRESH):
                    j, r, c = refreshed(u)[lu // NC], lu // NC, lu % NC
                    act.wait_ge(unit_ready, NT * i + lu + 1)
                    act.activation(expo[:, j, c * CH:(c + 1) * CH], banks[:, 4 + lu % 3, :], ACT.Exp,
                                   bias=expbias[:, j:j + 1], accum_out=parts[:, r, c:c + 1]).then_inc(unit_done, 1)

            act.preload_act_table_set("natural_log_exp_and_others")
            with act.Fori(0, batches) as b:
                with act.Fori(0, heads) as h:
                    n = b * heads + h
                    project(n)
                    if general:
                        with act.Fori(0, ITERS) as it:
                            g = n * steps + 2 * it
                            for s in range(2):
                                exponentials(g + s)
                                log_totals(g + s)
                    else:
                        exponentials(2 * n)
                        log_totals(2 * n)
                        exponentials(2 * n + 1)
                        with act.Fori(0, FAST // 4) as q:
                            for u in range(4):
                                iteration(n * FAST + q * 4 + u, u)
                        for u in range(FAST % 4):
                            iteration(n * FAST + FAST // 4 * 4 + u, u)
                    act.wait_ge(out_made, n + 1)
                    act.activation(outT[:, :, :].rearrange("p c n -> p (c n)"), flat(banks, 0, 2),
                                   ACT.Copy, scale=1.0 / LIFT).then_inc(out_stored, 1)

        @block.scalar
        def _(act):
            with if_needed(act):
                scalar_program(act)

        def vector_program(dve):
            def project(n):
                dve.wait_ge(weights_loaded, 16 * WLOADS * (n + 1))
                dve.tensor_scalar(bq_scaled[:, :], bq_col[:, :], HD ** -0.5, None,
                                  ALU.mult).then_inc(bias_scaled, 1)
                dve.wait_ge(k_made, n + 1)
                dve.memset(crow[:, :], 0.0)
                dve.tensor_scalar(kk[:, :], flat(banks, NC, NC), bk_col[:, 0:1], None, ALU.add).then_inc(k_stored, 1)

            def maxima(g):
                for t in range(NT):
                    dve.wait_ge(logits_ready, NT * g + t + 1)
                    dve.tensor_reduce(negmax[:, t:t + 1], flat(banks, NC * (t % 2), NC), AX.X, ALU.max,
                                      negate=True).then_inc(max_ready, 1)
                    dve.wait_ge(max_ready, NT * g + t + 1)
                    dve.tensor_scalar(expbias[:, t:t + 1], negmax[:, t:t + 1], LN_LIFT, None,
                                      ALU.add).then_inc(bias_ready, 1)

            def potential(r, columns):
                dve.wait_ge(lntotal_ready, r + 1)
                dve.tensor_tensor(negpot[:, :], negmax[:, :], lntotal[:, :], ALU.subtract).then_inc(negpot_ready, 1)
                dve.wait_ge(row_made, r + 1)
                if columns:
                    last = dve.tensor_copy(crow[:, :], banks[:, 0, :])
                else:
                    for c in range(NC):
                        part = qq[32 * c:32 * c + 1, c * CH:(c + 1) * CH]
                        last = dve.tensor_tensor(part, part, banks[32 * c:32 * c + 1, 0, :], ALU.add)
                last.then_inc(row_stored, 1)

            def iteration(i, wdone, u):
                dve.wait_ge(qbroad_ready, i + 1)
                tiles = order(u)

                def inverse(k):
                    j = tiles[k][0]
                    dve.wait_ge(sum_done, NT * i + k + 1)
                    dve.reciprocal(w[:, j:j + 1], total[:, u % 2, j:j + 1]).then_inc(w_ready, 1)

                for k, (j, r) in enumerate(tiles):
                    if r is None:
                        dve.scalar_tensor_tensor(
                            out=expo[:, j, :], in0=expo[:, j, :], scalar=FLOOR,
                            in1=flat(banks, 0, NC), op0=ALU.max, op1=ALU.mult,
                            accum_out=total[:, u % 2, j:j + 1]).then_inc(sum_done, 1)
                    else:
                        dve.wait_ge(unit_done, NT * i + NC * (r + 1))
                        dve.tensor_reduce(total[:, u % 2, j:j + 1], parts[:, r, :], AX.X,
                                          ALU.add).then_inc(sum_done, 1)
                    if k >= 1:
                        inverse(k - 1)
                inverse(NT - 1)

            if not general:
                dve.memset(least[:, :], 1.0).then_inc(least_ready, 1)
            with dve.Fori(0, batches) as b:
                with dve.Fori(0, heads) as h:
                    n = b * heads + h
                    project(n)
                    if general:
                        with dve.Fori(0, ITERS) as it:
                            g = n * steps + 2 * it
                            for s in range(2):
                                maxima(g + s)
                                potential(g + s, s == 1)
                    else:
                        maxima(2 * n)
                        potential(n, False)
                        maxima(2 * n + 1)
                    dve.wait_ge(exp_done, NT * steps * (n + 1))
                    if not general:
                        dve.memset(banks[:, 7, :], 1.0)
                    inverse_of = dve.reciprocal(w[:, :], total[:, 1, :])
                    inverse_of.then_inc(w_ready, NT)
                    if not general:
                        dve.wait_ge(lnrow_ready, n * FAST + 1)
                        dve.tensor_reduce(least[:, 1:2], banks[:, 7, :], AX.X, ALU.min).then_inc(least_ready, 1)
                        dve.wait_ge(least_ready, 2 * n + 2)
                        dve.tensor_tensor(least[:, 0:1], least[:, 0:1], least[:, 1:2], ALU.min).then_inc(least_ready, 1)
                        with dve.Fori(0, FAST // 4) as q:
                            for u in range(4):
                                iteration(n * FAST + q * 4 + u, 0, u)
                        for u in range(FAST % 4):
                            iteration(n * FAST + FAST // 4 * 4 + u, 0, u)
                        dve.wait_ge(w_ready, WPER * (n + 1))
                    else:
                        dve.wait_ge(w_ready, WPER * (n + 1))
                    dve.tensor_scalar(wlift[:, :], w[:, :], LIFT, None, ALU.mult).then_inc(wlast_ready, 1)
                    dve.wait_ge(wlast_ready, n + 1)
                    dve.tensor_tensor(vals[:, :, :], vals[:, :, :],
                                      wlift[:, :].unsqueeze(2).broadcast_to([P, NT, HD]),
                                      ALU.mult).then_inc(v_scaled, 1)
                    for j in (range(NT) if general else refreshed(FAST % 4 - 1)):
                        dve.tensor_scalar(expo[:, j, :], expo[:, j, :], FLOOR, None,
                                          ALU.max).then_inc(floored, 1)

        @block.vector
        def _(dve):
            with if_needed(dve):
                vector_program(dve)

        def gpsimd_program(pool):
            pool.memset(ones[:, :], 1.0).then_inc(const_ready, 1)
            pool.memset(sel[:, :, :], 0.0).then_inc(const_ready, 1)
            pool.memset(ident[:, :], 0.0).then_inc(const_ready, 1)
            pool.wait_ge(const_ready, 3)
            for c in range(NC):
                pool.memset(sel[32 * c:32 * c + 1, c, :], 1.0).then_inc(const_ready, 1)
            pool.wait_ge(const_ready, 3 + NC)
            pool.affine_select(out=ident[:, :], in_=ident[:, :], compare_op=ALU.not_equal, fill=1.0, base=0,
                               pattern=[[-1, P]], channel_multiplier=1).then_inc(const_ready, 1)

            def iteration(i, u):
                pool.wait_ge(lnrow_ready, i + 1)
                for c in range(NC):
                    part = qq[32 * c:32 * c + 1, c * CH:(c + 1) * CH]
                    pool.tensor_tensor(part, part, lnrow[32 * c:32 * c + 1, :], ALU.subtract).then_inc(rrow_ready, 1)
                pool.wait_ge(rrow_ready, NC * (i + 1))
                pool.wait_ge(oldtotal_ready, i + 1)
                group = slice(REFRESH * u, REFRESH * (u + 1))
                pool.tensor_tensor(expbias[:, group], expbias[:, group], lntotal[:, group],
                                   ALU.subtract).then_inc(expbias_ready, 1)

            if not general:
                with pool.Fori(0, batches) as b:
                    with pool.Fori(0, heads) as h:
                        n = b * heads + h
                        with pool.Fori(0, FAST // 4) as q:
                            for u in range(4):
                                iteration(n * FAST + q * 4 + u, u)
                        for u in range(FAST % 4):
                            iteration(n * FAST + FAST // 4 * 4 + u, u)

        @block.gpsimd
        def _(pool):
            with if_needed(pool):
                gpsimd_program(pool)


TG = 512
GT = TG // P
DM = 128
DI = 2
NS = 16
DR = 8
NE = 8
HF = 4
TAPS = 4
EPS_LN = 1e-5
EPS_ABSMEAN = 1e-6


def mamba_and_ffns(nc, d, xn1_T, partial, batches=BATCHES, groups=SEQ // TG):
    with ExitStack() as ctx:
        def sb(name, shape, dt=F32):
            return ctx.enter_context(nc.sbuf_tensor("m_" + name, shape, dt))

        def sem(name):
            return ctx.enter_context(nc.semaphore("m_" + name))

        in_w = sb("in_w", [P, 2 * DI * P])
        conv_w = sb("conv_w", [P, DI, TAPS])
        conv_b = sb("conv_b", [P, DI])
        xproj_w = sb("xproj_w", [P, DI, DR + 2 * NS])
        dt_w = sb("dt_w", [DR, DI * P])
        dt_b = sb("dt_b", [P, DI])
        a_log = sb("a_log", [P, DI, NS])
        neg_a = sb("neg_a", [P, DI, NS])
        a_exp = sb("a_exp", [P, DI, NS])
        d_skip = sb("d_skip", [P, DI])
        out_w = sb("out_w", [P, DI, DM])
        router_w = sb("router_w", [P, NE])
        router_b = sb("router_b", [P, NE])
        sw1, sw3 = sb("sw1", [P, 2 * P]), sb("sw3", [P, 2 * P])
        sw2 = sb("sw2", [P, 2, DM])
        ew1, ew2 = sb("ew1", [P, NE, P]), sb("ew2", [P, NE, DM])
        fc_w, proj_w = sb("fc_w", [P, HF * P]), sb("proj_w", [P, HF * DM])
        tern = sb("tern", [P, HF * P])
        gsum = sb("gsum", [P, 2])
        half_gamma = sb("half_gamma", [P, 4])
        ln_w, ln_b = sb("ln_w", [P, HF]), sb("ln_b", [P, HF])
        pick = sb("pick", [DR + 2 * NS, 2 * NS, P])
        ident, ones = sb("ident", [P, P]), sb("ones", [P, P])
        falling = sb("falling", [P, GT, NE])

        x_tok, xn_tok = sb("x_tok", [P, GT, DM]), sb("xn_tok", [P, GT, DM])
        stats, moments = sb("stats", [P, GT, 6]), sb("moments", [P, GT, 2])
        veps, std, rstd = sb("veps", [P, GT]), sb("std", [P, GT]), sb("rstd", [P, GT])
        xnT = sb("xnT", [P, TG])
        xpad = sb("xpad", [P, DI, TAPS - 1 + TG])
        conv = sb("conv", [P, DI, TG])
        u, gate = sb("u", [P, DI, TG]), sb("gate", [P, DI, TG])
        xdb = sb("xdb", [DR + 2 * NS, TG])
        z, t_exp, w1p, lnw = sb("z", [P, DI, TG]), sb("t_exp", [P, DI, TG]), sb("w1p", [P, DI, TG]), sb("lnw", [P, DI, TG])
        delta, du = sb("delta", [P, DI, TG]), sb("du", [P, DI, TG])
        da = sb("da", [P, 4, TG])
        dbu = sb("dbu", [P, 2, TG])
        hist = sb("hist", [P, NS, DI, TG])
        state = sb("state", [P, NS, DI])
        hc = sb("hc", [P, 4, TG])
        y = sb("y", [P, DI, TG])
        yg = sb("yg", [P, DI, TG])
        s1 = sb("s1", [P, 2, TG])
        shared = sb("shared", [P, 2, TG])
        score, sel = sb("score", [P, GT, NE]), sb("sel", [P, GT, NE])
        top, eq, hot1, hot2 = sb("top", [P, GT]), sb("eq", [P, GT, NE]), sb("hot1", [P, GT, NE]), sb("hot2", [P, GT, NE])
        denom, inv, isbig, comb = sb("denom", [P, GT]), sb("inv", [P, GT]), sb("isbig", [P, GT]), sb("comb", [P, GT, NE])
        he = sb("he", [P, 2, TG])
        acc = sb("acc", [P, GT, DM])
        x1 = sb("x1", [P, GT, DM])
        hg, hn = (hist[:, :, :, :].rearrange("p n c t -> p (n c) t")[:, GT * i:GT * (i + 1), :] for i in range(2))
        hT = sb("hT", [P, 2, HF, P])
        fin = sb("fin", [P, GT, DM])
        pause = sb("pause", [P, 1])
        ps = ctx.enter_context(nc.psum_tensor("m_ps", [P, 8, CH], F32))

        sp_steps = sem("sp_steps")
        loaded, const_ready, ternary = sem("loaded"), sem("const_ready"), sem("ternary")
        asum_ready, gtotal_made, aexp_ready = sem("asum_ready"), sem("gtotal_made"), sem("aexp_ready")
        names = ("x_loaded var0 std0 xn0_ready tr0_made xnT_stored inproj_made xpad_stored conv_ready u_ready "
                 "gate_ready xdb_made xdb_stored dt_made z_ready t_ready w1p_ready lnw_ready du_ready y_start "
                 "b_made c_made da_ready b_used hc_ready hist_kept y_ready yg_ready shared_made s1_ready "
                 "shared_ready router_made score_ready comb_ready eh_made he_ready ey_made ey_used "
                 "mix_made x1_ready var1 std1 xn1_ready tr1_made xn1T_stored xn1T_written fc_made hg_ready "
                 "var2 std2 hn_ready hT_made hT_stored ff_made fin_ready fin_written dve_order pool_order act_order")
        S = {name: sem(name) for name in names.split()}

        LOADS = [(in_w[:, :], d["in_w"]), (conv_w[:, :, :], d["conv_w"]), (conv_b[:, :], d["conv_b"]),
                 (xproj_w[:, :, :], d["xproj_w"]), (dt_w[:, :], d["dt_w"]), (dt_b[:, :], d["dt_b"]),
                 (a_log[:, :, :], d["a_log"]), (d_skip[:, :], d["d_skip"]), (out_w[:, :, :], d["out_w"]),
                 (router_w[:, :], d["router_w"]), (router_b[:, :], d["router_b"]), (sw1[:, :], d["sw1"]),
                 (sw3[:, :], d["sw3"]), (sw2[:, :, :], d["sw2"]), (ew1[:, :, :], d["ew1"]), (ew2[:, :, :], d["ew2"]),
                 (fc_w[:, :], d["fc_w"]), (proj_w[:, :], d["proj_w"]), (ln_w[:, :], d["ln_w"]), (ln_b[:, :], d["ln_b"]),
                 (pick[:, :, :], d["pick"])]
        ALL_LOADED = 16 * len(LOADS)

        def flat(ap):
            return ap.rearrange("p a n -> p (a n)")

        block = ctx.enter_context(nc.Block())

        class Order:

            def __init__(self, eng, name, per_group):
                self.eng, self.sem, self.per, self.base, self.n = eng, S[name], per_group, 0, 0

            def start(self, g):
                self.base, self.n = g * self.per, 0

            def __call__(self, ins):
                self.n += 1
                assert self.n <= self.per
                ins.then_inc(self.sem, 1)
                self.eng.wait_ge(self.sem, self.base + self.n)

            def end(self):
                assert self.n == self.per, self.n

        @block.sync
        def _(sp):
            for dst, src in LOADS:
                sp.dma_start(dst, src).then_inc(loaded, 16)
            with sp.Fori(0, batches) as b:
                with sp.Fori(0, groups) as q:
                    g = b * groups + q
                    row = b * SEQ + q * TG
                    sp.dma_start(x_tok[:, :, :], d["x"][bass.ds(row, TG), :].rearrange("(k p) n -> p k n", p=P)
                                 ).then_inc(S["x_loaded"], 16)
                    sp.wait_ge(S["xn1T_stored"], g + 1)
                    sp.sem_inc(sp_steps, 1)
                    sp.dma_start(xn1_T[:, bass.ds(row, TG)], xnT[:, :]).then_inc(S["xn1T_written"], 16)
                    sp.wait_ge(S["fin_ready"], g + 1)
                    sp.sem_inc(sp_steps, 1)
                    sp.dma_start(partial[bass.ds(row, TG), :].rearrange("(k p) n -> p k n", p=P),
                                 fin[:, :, :]).then_inc(S["fin_written"], 16)
                    sp.wait_ge(S["xn1T_written"], 16 * (g + 1))
                    sp.wait_ge(S["fin_written"], 16 * (g + 1))
                    sp.sem_inc(sp_steps, 1)

        @block.tensor
        def _(pe):
            def project(g, k):
                pe.wait_ge(S["hT_stored"], g * GT + k + 1)
                for j in range(HF):
                    last = pe.matmul(ps[:, 6, k * DM:(k + 1) * DM], hT[:, k % 2, j, :], proj_w[:, j * DM:(j + 1) * DM],
                                     start=(j == 0), stop=(j == HF - 1))
                last.then_inc(S["ff_made"], 1)

            pe.wait_ge(const_ready, 3)
            pe.wait_ge(loaded, ALL_LOADED)
            pe.wait_ge(asum_ready, 2)
            pe.matmul(ps[:, 0, 0:2], ones[:, :], gsum[:, :], start=True, stop=True).then_inc(gtotal_made, 1)
            pe.wait_ge(ternary, 4)
            with pe.Fori(0, batches) as b:
                with pe.Fori(0, groups) as q:
                    g = b * groups + q
                    now = g + 1
                    pe.wait_ge(S["xn0_ready"], now)
                    for k in range(GT):
                        last = pe.transpose(ps[:, 0, k * P:(k + 1) * P], xn_tok[:, k, :], ident[:, :])
                    last.then_inc(S["tr0_made"], 1)
                    pe.wait_ge(S["xnT_stored"], now)
                    for j in range(2 * DI):
                        last = pe.matmul(ps[:, 1 + j, :], in_w[:, j * P:(j + 1) * P], xnT[:, :], start=True, stop=True)
                    last.then_inc(S["inproj_made"], 1)
                    for k in range(GT):
                        last = pe.matmul(ps[:, 7, k * NE:(k + 1) * NE], xnT[:, k * P:(k + 1) * P], router_w[:, :],
                                         start=True, stop=True)
                    last.then_inc(S["router_made"], 1)
                    pe.wait_ge(S["u_ready"], now)
                    for ct in range(DI):
                        last = pe.matmul(ps[0:DR + 2 * NS, 5, :], xproj_w[:, ct, :], u[:, ct, :],
                                         start=(ct == 0), stop=(ct == DI - 1))
                    last.then_inc(S["xdb_made"], 1)
                    pe.wait_ge(S["xdb_stored"], now)
                    pe.wait_ge(S["gate_ready"], now)
                    for ct in range(DI):
                        last = pe.matmul(ps[:, 3 + ct, :], dt_w[:, ct * P:(ct + 1) * P], xdb[0:DR, :],
                                         start=True, stop=True)
                    last.then_inc(S["dt_made"], 1)
                    pe.wait_ge(S["z_ready"], now)
                    for n in range(NS):
                        if n >= 2:
                            pe.wait_ge(S["b_used"], g * NS + n - 1)
                        pe.matmul(ps[:, 2 * (n % 2), :], pick[:, n, :], xdb[:, :], start=True,
                                  stop=True).then_inc(S["b_made"], 1)
                        if n >= 2:
                            pe.wait_ge(S["hc_ready"], g * (NS * DI) + DI * (n - 1))
                        pe.matmul(ps[:, 1 + 2 * (n % 2), :], pick[:, NS + n, :], xdb[:, :], start=True,
                                  stop=True).then_inc(S["c_made"], 1)
                    pe.wait_ge(S["score_ready"], now)
                    for j in range(2):
                        pe.matmul(ps[:, 4 + j, :], sw1[:, j * P:(j + 1) * P], xnT[:, :], start=True, stop=True)
                    for j in range(2):
                        last = pe.matmul(ps[:, 6 + j, :], sw3[:, j * P:(j + 1) * P], xnT[:, :], start=True, stop=True)
                    last.then_inc(S["shared_made"], 1)
                    pe.wait_ge(S["shared_ready"], now)
                    for e in range(NE + 1):
                        if e < NE:
                            if e >= 2:
                                pe.wait_ge(S["he_ready"], g * NE + e - 1)
                            pe.matmul(ps[:, 4 + e % 2, :], ew1[:, e, :], xnT[:, :], start=True,
                                      stop=True).then_inc(S["eh_made"], 1)
                        if e >= 1:
                            f = e - 1
                            pe.wait_ge(S["he_ready"], g * NE + f + 1)
                            if f >= 2:
                                pe.wait_ge(S["ey_used"], g * NE + f - 1)
                            for k in range(GT):
                                last = pe.matmul(ps[:, 6 + f % 2, k * DM:(k + 1) * DM], he[:, f % 2, k * P:(k + 1) * P],
                                                 ew2[:, f, :], start=True, stop=True)
                            last.then_inc(S["ey_made"], 1)
                    pe.wait_ge(S["yg_ready"], now)
                    for k in range(GT):
                        out, tok = ps[:, 0, k * DM:(k + 1) * DM], slice(k * P, (k + 1) * P)
                        for j in range(DI):
                            pe.matmul(out, yg[:, j, tok], out_w[:, j, :], start=(j == 0), stop=False)
                        for j in range(2):
                            last = pe.matmul(out, shared[:, j, tok], sw2[:, j, :], start=False, stop=(j == 1))
                    last.then_inc(S["mix_made"], 1)
                    pe.wait_ge(S["xn1_ready"], now)
                    for k in range(GT):
                        last = pe.transpose(ps[:, 1, k * P:(k + 1) * P], xn_tok[:, k, :], ident[:, :])
                    last.then_inc(S["tr1_made"], 1)
                    pe.wait_ge(S["xn1T_stored"], now)
                    for k in range(GT):
                        if k >= 2:
                            pe.wait_ge(S["hg_ready"], g * GT + k - 1)
                        pe.matmul(ps[:, 2 + k % 2, :], xnT[:, k * P:(k + 1) * P], tern[:, :], start=True,
                                  stop=True).then_inc(S["fc_made"], 1)
                    pe.wait_ge(S["hn_ready"], now)
                    for k in range(GT):
                        if k >= 2:
                            pe.wait_ge(S["hT_stored"], g * GT + k - 1)
                        for j in range(HF):
                            last = pe.transpose(ps[:, 4 + k % 2, j * P:(j + 1) * P], hn[:, k, j * P:(j + 1) * P],
                                                ident[:, :])
                        last.then_inc(S["hT_made"], 1)
                        if k >= 1:
                            project(g, k - 1)
                    project(g, GT - 1)

        @block.scalar
        def _(act):
            act.wait_ge(loaded, ALL_LOADED)
            act.activation(a_exp[:, :, :], a_log[:, :, :], ACT.Exp).then_inc(aexp_ready, 1)
            with act.Fori(0, batches) as b:
                with act.Fori(0, groups) as q:
                    g = b * groups + q
                    now = g + 1
                    act.wait_ge(S["var0"], now)
                    act.activation(std[:, :], veps[:, :], ACT.Sqrt).then_inc(S["std0"], 1)
                    act.wait_ge(S["tr0_made"], now)
                    act.activation(xnT[:, :], ps[:, 0, :], ACT.Copy).then_inc(S["xnT_stored"], 1)
                    act.wait_ge(S["inproj_made"], now)
                    act.activation(xpad[:, :, TAPS - 1:], ps[:, 1:3, :], ACT.Copy).then_inc(S["xpad_stored"], 1)
                    act.activation(gate[:, :, :], ps[:, 3:5, :], ACT.Silu).then_inc(S["gate_ready"], 1)
                    act.wait_ge(S["conv_ready"], now)
                    act.activation(u[:, :, :], conv[:, :, :], ACT.Silu).then_inc(S["u_ready"], 1)
                    act.wait_ge(S["router_made"], now)
                    act.activation(flat(score[:, :, :]), ps[:, 7, 0:GT * NE], ACT.Sigmoid).then_inc(S["score_ready"], 1)
                    act.wait_ge(S["xdb_made"], now)
                    act.activation(xdb[:, :], ps[0:DR + 2 * NS, 5, :], ACT.Copy).then_inc(S["xdb_stored"], 1)
                    act.wait_ge(S["z_ready"], now)
                    act.activation(t_exp[:, :, :], w1p[:, :, :], ACT.Exp, scale=-1.0).then_inc(S["t_ready"], 1)
                    act.wait_ge(S["w1p_ready"], now)
                    act.activation(lnw[:, :, :], w1p[:, :, :], ACT.Ln).then_inc(S["lnw_ready"], 1)
                    act.wait_ge(S["du_ready"], now)
                    for n in range(NS):
                        for ct in range(DI):
                            m = n * DI + ct
                            if m >= 4:
                                act.wait_ge(S["hc_ready"], g * (NS * DI) + m - 3)
                            act.activation(da[:, m % 4, :], delta[:, ct, :], ACT.Exp,
                                           scale=neg_a[:, ct, n:n + 1]).then_inc(S["da_ready"], 1)
                    act.wait_ge(S["shared_made"], now)
                    act.activation(s1[:, :, :], ps[:, 4:6, :], ACT.Silu).then_inc(S["s1_ready"], 1)
                    for e in range(NE):
                        act.wait_ge(S["eh_made"], g * NE + e + 1)
                        if e >= 2:
                            act.wait_ge(S["ey_made"], g * NE + e - 1)
                        act.activation(he[:, e % 2, :], ps[:, 4 + e % 2, :], ACT.Gelu).then_inc(S["he_ready"], 1)
                    act.wait_ge(S["var1"], now)
                    act.activation(std[:, :], veps[:, :], ACT.Sqrt).then_inc(S["std1"], 1)
                    act.wait_ge(S["tr1_made"], now)
                    act.activation(xnT[:, :], ps[:, 1, :], ACT.Copy).then_inc(S["xn1T_stored"], 1)
                    for k in range(GT):
                        act.wait_ge(S["fc_made"], g * GT + k + 1)
                        act.activation(hg[:, k, :], ps[:, 2 + k % 2, :], ACT.Gelu).then_inc(S["hg_ready"], 1)
                    act.wait_ge(S["var2"], now)
                    act.activation(std[:, :], veps[:, :], ACT.Sqrt).then_inc(S["std2"], 1)

        @block.vector
        def _(dve):
            link = Order(dve, "dve_order", 75)

            def moments_of(source, var_sem):
                for k in range(GT):
                    ins = dve.bn_stats(stats[:, k, :], source[:, k, :])
                link(ins)
                dve.memset(pause[:, :], 0.0)
                for k in range(GT):
                    ins = dve.bn_aggr(moments[:, k, :], stats[:, k, :])
                link(ins)
                dve.tensor_scalar(veps[:, :], moments[:, :, 1], EPS_LN, None, ALU.add).then_inc(S[var_sem], 1)

            def normalised(out, source, std_sem, ready, now):
                dve.wait_ge(S[std_sem], now)
                link(dve.reciprocal(rstd[:, :], std[:, :]))
                for k in range(GT):
                    ins = dve.tensor_scalar(out[:, k, :], source[:, k, :], moments[:, k, 0:1], rstd[:, k:k + 1],
                                            ALU.subtract, ALU.mult)
                ins.then_inc(S[ready], 1)

            dve.wait_ge(loaded, ALL_LOADED)
            dve.tensor_reduce(gsum[:, 0:1], fc_w[:, :], AX.X, ALU.add, apply_absolute_value=True).then_inc(asum_ready, 1)
            dve.tensor_reduce(gsum[:, 1:2], proj_w[:, :], AX.X, ALU.add, apply_absolute_value=True).then_inc(asum_ready, 1)
            dve.wait_ge(gtotal_made, 1)
            dve.tensor_scalar(half_gamma[:, 0:2], ps[:, 0, 0:2], 1.0 / (HF * P * DM), EPS_ABSMEAN, ALU.mult,
                              ALU.add).then_inc(ternary, 1)
            dve.wait_ge(ternary, 1)
            dve.tensor_scalar(half_gamma[:, 2:4], half_gamma[:, 0:2], -0.5, None, ALU.mult).then_inc(ternary, 1)
            dve.wait_ge(ternary, 2)
            dve.tensor_scalar(half_gamma[:, 0:2], half_gamma[:, 2:4], -1.0, None, ALU.mult).then_inc(ternary, 1)
            dve.wait_ge(ternary, 3)
            dve.tensor_scalar(tern[:, :], fc_w[:, :], half_gamma[:, 2:3], None, ALU.is_lt)
            dve.tensor_scalar(hn[:, 0, :], proj_w[:, :], half_gamma[:, 3:4], None, ALU.is_lt).then_inc(asum_ready, 1)
            dve.wait_ge(asum_ready, 3)
            dve.scalar_tensor_tensor(out=tern[:, :], in0=fc_w[:, :], scalar=half_gamma[:, 0:1], in1=tern[:, :],
                                     op0=ALU.is_gt, op1=ALU.subtract)
            dve.scalar_tensor_tensor(out=proj_w[:, :], in0=proj_w[:, :], scalar=half_gamma[:, 1:2], in1=hn[:, 0, :],
                                     op0=ALU.is_gt, op1=ALU.subtract).then_inc(ternary, 1)
            dve.wait_ge(aexp_ready, 1)
            dve.tensor_scalar(neg_a[:, :, :], a_exp[:, :, :], -1.0, None, ALU.mult)
            for e in range(NE):
                dve.memset(falling[:, :, e:e + 1], float(NE - e))
            with dve.Fori(0, batches) as b:
                dve.memset(xpad[:, :, 0:TAPS - 1], 0.0)
                dve.memset(state[:, :, :], 0.0)
                with dve.Fori(0, groups) as q:
                    g = b * groups + q
                    now = g + 1
                    link.start(g)
                    dve.wait_ge(S["x_loaded"], 16 * now)
                    moments_of(x_tok, "var0")
                    normalised(xn_tok, x_tok, "std0", "xn0_ready", now)
                    dve.wait_ge(S["xpad_stored"], now)
                    for ct in range(DI):
                        ins = dve.tensor_scalar(conv[:, ct, :], xpad[:, ct, 0:TG], conv_w[:, ct, 0:1],
                                                conv_b[:, ct:ct + 1], ALU.mult, ALU.add)
                    link(ins)
                    for tap in range(1, TAPS):
                        for ct in range(DI):
                            ins = dve.scalar_tensor_tensor(out=conv[:, ct, :], in0=xpad[:, ct, tap:tap + TG],
                                                           scalar=conv_w[:, ct, tap:tap + 1], in1=conv[:, ct, :],
                                                           op0=ALU.mult, op1=ALU.add)
                        if tap < TAPS - 1:
                            link(ins)
                    ins.then_inc(S["conv_ready"], 1)
                    link(dve.tensor_copy(xpad[:, :, 0:TAPS - 1], xpad[:, :, TG:TG + TAPS - 1]))
                    dve.wait_ge(S["dt_made"], now)
                    for ct in range(DI):
                        ins = dve.tensor_scalar(z[:, ct, :], ps[:, 3 + ct, :], dt_b[:, ct:ct + 1], dt_b[:, ct:ct + 1],
                                                ALU.add, ALU.add)
                    link(ins)
                    link(dve.tensor_scalar(w1p[:, :, :], z[:, :, :], -1.0, None, ALU.mult))
                    dve.tensor_tensor(w1p[:, :, :], w1p[:, :, :], z[:, :, :], ALU.max).then_inc(S["z_ready"], 1)
                    dve.wait_ge(S["t_ready"], now)
                    dve.tensor_scalar(w1p[:, :, :], t_exp[:, :, :], 1.0, None, ALU.add).then_inc(S["w1p_ready"], 1)
                    dve.wait_ge(S["w1p_ready"], now)
                    link(dve.scalar_tensor_tensor(out=t_exp[:, :, :], in0=w1p[:, :, :], scalar=-1.0, in1=t_exp[:, :, :],
                                                  op0=ALU.add, op1=ALU.subtract))
                    dve.wait_ge(S["lnw_ready"], now)
                    link(dve.tensor_tensor(t_exp[:, :, :], lnw[:, :, :], t_exp[:, :, :], ALU.subtract))
                    link(dve.scalar_tensor_tensor(out=delta[:, :, :], in0=z[:, :, :], scalar=0.0, in1=t_exp[:, :, :],
                                                  op0=ALU.max, op1=ALU.add))
                    dve.tensor_tensor(du[:, :, :], delta[:, :, :], u[:, :, :], ALU.mult).then_inc(S["du_ready"], 1)
                    dve.wait_ge(S["du_ready"], now)
                    for n in range(NS):
                        for ct in range(DI):
                            m = n * DI + ct
                            if ct == 0:
                                dve.wait_ge(S["b_made"], g * NS + n + 1)
                            ins = dve.tensor_tensor(dbu[:, ct, :], du[:, ct, :], ps[:, 2 * (n % 2), :], ALU.mult)
                        ins.then_inc(S["b_used"], 1)
                        dve.wait_ge(S["b_used"], g * NS + n + 1)
                        for ct in range(DI):
                            m = n * DI + ct
                            dve.wait_ge(S["da_ready"], g * (NS * DI) + m + 1)
                            link(dve.tensor_tensor_scan(hist[:, n, ct, :], da[:, m % 4, :], dbu[:, ct, :],
                                                        state[:, n, ct:ct + 1], ALU.mult, ALU.add))
                            if m >= 4:
                                dve.wait_ge(S["y_ready"], g * (NS * DI) + m - 3)
                            if ct == 0:
                                dve.wait_ge(S["c_made"], g * NS + n + 1)
                            dve.tensor_tensor(hc[:, m % 4, :], hist[:, n, ct, :], ps[:, 1 + 2 * (n % 2), :],
                                              ALU.mult).then_inc(S["hc_ready"], 1)
                    link(dve.tensor_copy(state[:, :, :], hist[:, :, :, TG - 1]))
                    dve.wait_ge(S["s1_ready"], now)
                    dve.tensor_tensor(shared[:, :, :], s1[:, :, :], ps[:, 6:8, :], ALU.mult).then_inc(S["shared_ready"], 1)
                    dve.wait_ge(S["score_ready"], now)
                    link(dve.tensor_tensor(sel[:, :, :], score[:, :, :],
                                           router_b[:, :].unsqueeze(1).broadcast_to([P, GT, NE]), ALU.add))
                    for hot in (hot1, hot2):
                        link(dve.tensor_reduce(top[:, :], sel[:, :, :], AX.X, ALU.max))
                        wide = top[:, :].unsqueeze(2).broadcast_to([P, GT, NE])
                        link(dve.tensor_tensor(eq[:, :, :], sel[:, :, :], wide, ALU.is_equal))
                        link(dve.tensor_tensor(eq[:, :, :], eq[:, :, :], falling[:, :, :], ALU.mult))
                        link(dve.tensor_reduce(top[:, :], eq[:, :, :], AX.X, ALU.max))
                        link(dve.tensor_tensor(hot[:, :, :], falling[:, :, :], wide, ALU.is_equal))
                        if hot is hot1:
                            link(dve.scalar_tensor_tensor(out=sel[:, :, :], in0=hot1[:, :, :], scalar=-3.0e38,
                                                          in1=sel[:, :, :], op0=ALU.mult, op1=ALU.add))
                    link(dve.tensor_tensor(hot1[:, :, :], hot1[:, :, :], hot2[:, :, :], ALU.add))
                    link(dve.tensor_tensor(eq[:, :, :], hot1[:, :, :], score[:, :, :], ALU.mult))
                    link(dve.tensor_reduce(denom[:, :], eq[:, :, :], AX.X, ALU.add))
                    link(dve.tensor_scalar(isbig[:, :], denom[:, :], 1e-9, None, ALU.is_gt))
                    link(dve.tensor_scalar(inv[:, :], denom[:, :], 1e-9, None, ALU.add))
                    link(dve.reciprocal(denom[:, :], inv[:, :]))
                    link(dve.tensor_tensor(denom[:, :], denom[:, :], isbig[:, :], ALU.mult))
                    link(dve.tensor_tensor(eq[:, :, :], eq[:, :, :], denom[:, :].unsqueeze(2).broadcast_to([P, GT, NE]),
                                           ALU.mult))
                    link(dve.tensor_scalar(isbig[:, :], isbig[:, :], -0.5, 0.5, ALU.mult, ALU.add))
                    link(dve.tensor_tensor(hot2[:, :, :], hot1[:, :, :], isbig[:, :].unsqueeze(2).broadcast_to([P, GT, NE]),
                                           ALU.mult))
                    link(dve.tensor_tensor(comb[:, :, :], eq[:, :, :], hot2[:, :, :], ALU.add))
                    dve.wait_ge(S["y_ready"], (g + 1) * NS * DI)
                    dve.tensor_tensor(yg[:, :, :], y[:, :, :], gate[:, :, :], ALU.mult).then_inc(S["yg_ready"], 1)
                    for e in range(NE):
                        dve.wait_ge(S["ey_made"], g * NE + e + 1)
                        if e:
                            dve.wait_ge(S["ey_used"], g * NE + e)
                        for k in range(GT):
                            base = x_tok if e == 0 else acc
                            ins = dve.scalar_tensor_tensor(out=acc[:, k, :], in0=ps[:, 6 + e % 2, k * DM:(k + 1) * DM],
                                                           scalar=comb[:, k, e:e + 1], in1=base[:, k, :],
                                                           op0=ALU.mult, op1=ALU.add)
                        ins.then_inc(S["ey_used"], 1)
                    dve.wait_ge(S["ey_used"], (g + 1) * NE)
                    dve.wait_ge(S["mix_made"], now)
                    link(dve.tensor_tensor(flat(x1[:, :, :]), flat(acc[:, :, :]), ps[:, 0, :], ALU.add))
                    moments_of(x1, "var1")
                    normalised(xn_tok, x1, "std1", "xn1_ready", now)
                    dve.wait_ge(S["hg_ready"], (g + 1) * GT)
                    moments_of(hg, "var2")
                    normalised(hn, hg, "std2", "hn_ready", now)
                    for k in range(GT):
                        dve.wait_ge(S["hT_made"], g * GT + k + 1)
                        if k >= 2:
                            dve.wait_ge(S["ff_made"], g * GT + k - 1)
                        for j in range(HF):
                            ins = dve.tensor_scalar(hT[:, k % 2, j, :], ps[:, 4 + k % 2, j * P:(j + 1) * P],
                                                    ln_w[:, j:j + 1], ln_b[:, j:j + 1], ALU.mult, ALU.add)
                        ins.then_inc(S["hT_stored"], 1)
                    dve.wait_ge(S["ff_made"], (g + 1) * GT)
                    dve.tensor_tensor(flat(fin[:, :, :]), flat(x1[:, :, :]), ps[:, 6, :], ALU.add).then_inc(S["fin_ready"], 1)
                    link.end()

        @block.gpsimd
        def _(pool):
            pool.memset(ones[:, :], 1.0).then_inc(const_ready, 1)
            pool.memset(ident[:, :], 0.0).then_inc(const_ready, 1)
            pool.wait_ge(const_ready, 2)
            pool.affine_select(out=ident[:, :], in_=ident[:, :], compare_op=ALU.not_equal, fill=1.0, base=0,
                               pattern=[[-1, P]], channel_multiplier=1).then_inc(const_ready, 1)
            with pool.Fori(0, batches) as b:
                with pool.Fori(0, groups) as q:
                    g = b * groups + q
                    now = g + 1
                    pool.wait_ge(S["u_ready"], now)
                    pool.wait_ge(loaded, ALL_LOADED)
                    for ct in range(DI):
                        ins = pool.tensor_tensor(y[:, ct, :], u[:, ct, :],
                                                 d_skip[:, ct:ct + 1].broadcast_to([P, TG]), ALU.mult)
                    ins.then_inc(S["y_start"], 1)
                    pool.wait_ge(S["y_start"], now)
                    for m in range(NS * DI):
                        pool.wait_ge(S["hc_ready"], g * (NS * DI) + m + 1)
                        if m >= 2:
                            pool.wait_ge(S["y_ready"], g * (NS * DI) + m - 1)
                        pool.tensor_tensor(y[:, m % 2, :], y[:, m % 2, :], hc[:, m % 4, :],
                                           ALU.add).then_inc(S["y_ready"], 1)


def output_projection(nc, head_out, Wo, bo, partial, out, batches=BATCHES, groups=SEQ // TG):
    with ExitStack() as ctx:
        def sb(name, shape):
            return ctx.enter_context(nc.sbuf_tensor("o_" + name, shape, F32))

        def sem(name):
            return ctx.enter_context(nc.semaphore("o_" + name))

        wo = sb("wo", [P, 4, DM])
        bo_row, ones = sb("bo_row", [1, DM]), sb("ones", [1, P])
        heads_T = sb("heads_T", [P, 4, SEQ])
        base, done = sb("base", [P, NT, DM]), sb("done", [P, NT, DM])
        ps = ctx.enter_context(nc.psum_tensor("o_ps", [P, 4, CH], F32))
        w_loaded, ones_ready, loaded = sem("w_loaded"), sem("ones_ready"), sem("loaded")
        sp_steps = sem("sp_steps")
        made, added, stored = sem("made"), sem("added"), sem("stored")

        LOADS = 16 * 8

        block = ctx.enter_context(nc.Block())

        @block.sync
        def _(sp):
            sp.dma_start(wo[:, :, :], Wo).then_inc(w_loaded, 16)
            sp.dma_start(bo_row[:, :], bo).then_inc(w_loaded, 16)
            with sp.Fori(0, batches) as b:
                for c in range(4):
                    sp.dma_start(base[:, GT * c:GT * (c + 1), :], partial[bass.ds(b * SEQ + c * TG, TG), :].rearrange(
                        "(t p) n -> p t n", p=P)).then_inc(loaded, 16)
                for j in range(4):
                    sp.dma_start(heads_T[:, j, :], head_out[bass.ds(b * HEADS + 2 * j, 2), :, :].rearrange(
                        "a d n -> (a d) n")).then_inc(loaded, 16)
                for c in range(4):
                    sp.wait_ge(added, 4 * b + c + 1)
                    sp.sem_inc(sp_steps, 1)
                    sp.dma_start(out[bass.ds(b * SEQ + c * TG, TG), :].rearrange("(t p) n -> p t n", p=P),
                                 done[:, GT * c:GT * (c + 1), :]).then_inc(stored, 16)
                sp.wait_ge(stored, 64 * (b + 1))
                sp.sem_inc(sp_steps, 1)

        @block.tensor
        def _(pe):
            pe.wait_ge(w_loaded, 32)
            pe.wait_ge(ones_ready, 1)
            with pe.Fori(0, batches) as b:
                pe.wait_ge(loaded, LOADS * (b + 1))
                for t in range(NT):
                    dst = ps[:, t // GT, (t % GT) * DM:(t % GT + 1) * DM]
                    for j in range(4):
                        pe.matmul(dst, heads_T[:, j, t * P:(t + 1) * P], wo[:, j, :], start=(j == 0), stop=False)
                    last = pe.matmul(dst, ones[:, :], bo_row[:, :], start=False, stop=True)
                    if t % GT == GT - 1:
                        last.then_inc(made, 1)

        @block.vector
        def _(dve):
            dve.memset(ones[:, :], 1.0).then_inc(ones_ready, 1)
            with dve.Fori(0, batches) as b:
                dve.wait_ge(loaded, LOADS * (b + 1))
                for c in range(4):
                    dve.wait_ge(made, 4 * b + c + 1)
                    dve.tensor_tensor(done[:, GT * c:GT * (c + 1), :].rearrange("p t n -> p (t n)"), ps[:, c, :],
                                      base[:, GT * c:GT * (c + 1), :].rearrange("p t n -> p (t n)"),
                                      ALU.add).then_inc(added, 1)


def read_floor(nc, rowsum_floor, verdict):
    with ExitStack() as ctx:
        floors = ctx.enter_context(nc.sbuf_tensor("v_floors", [1, P], F32))
        floor = ctx.enter_context(nc.sbuf_tensor("v_floor", [1, 1], F32))
        loaded = ctx.enter_context(nc.semaphore("v_loaded"))
        judged = ctx.enter_context(nc.semaphore("v_judged"))
        block = ctx.enter_context(nc.Block())

        @block.sync
        def _(sp):
            sp.dma_start(floors[:, :], rowsum_floor.rearrange("p o -> o p")).then_inc(loaded, 16)

        @block.vector
        def _(dve):
            dve.wait_ge(loaded, 16)
            dve.tensor_reduce(floor[:, :], floors[:, :], AX.X, ALU.min).then_inc(judged, 1)
            dve.wait_ge(judged, 1)
            dve.tensor_scalar(verdict[:, :], floor[:, :], SAFE_ROWSUM, None, ALU.is_lt).then_inc(judged, 1)


def build(nc, d, out):
    xn1_T = nc.dram_tensor("xn1_T", (P, BATCHES * SEQ), F32, kind="Internal").ap()
    partial = nc.dram_tensor("partial", (BATCHES * SEQ, DM), F32, kind="Internal").ap()
    head_out = nc.dram_tensor("head_out", (BATCHES * HEADS, HD, SEQ), F32, kind="Internal").ap()
    rowsum_floor = nc.dram_tensor("rowsum_floor", (P, 1), F32, kind="Internal").ap()
    mamba_and_ffns(nc, d, xn1_T, partial)
    attention = (xn1_T, d["wq"], d["bq"], d["wk"], d["bk"], d["wv"], d["bv"], head_out, rowsum_floor)
    sinkhorn(nc, *attention, general=False)
    with nc.sbuf_tensor("verdict", [1, 1], I32) as verdict:
        read_floor(nc, rowsum_floor, verdict)
        sinkhorn(nc, *attention, general=True, verdict=verdict)
    output_projection(nc, head_out, d["wo"], d["bo"], partial, out)



def kernel(**inputs):
    import numpy as np
    import concourse.bacc as bacc
    from concourse.bass_utils import run_bass_kernel_spmd

    a = {k: np.ascontiguousarray(v) for k, v in inputs.items()}

    def by_partition(x):
        return x.reshape(-1, P, *x.shape[1:]).swapaxes(0, 1)

    def to_rows(x, ones_between=False):
        out = np.zeros((x.shape[0], HEADS, P), x.dtype)
        out[:, :, FEATURE_ROWS] = x.reshape(x.shape[0], HEADS, HD)
        if ones_between:
            out[:, :, ::32] = 1
        return out.reshape(x.shape[0], HEADS * P)

    f, m, t, s = "L0_ffn_", "L0_attn_", "L1_attn_", "L1_ffn_"
    pick = np.zeros((DR + 2 * NS, 2 * NS, P), np.float32)
    pick[DR + np.arange(2 * NS), np.arange(2 * NS)] = 1
    arrays = {
        "x": a[m + "hidden_states"].reshape(BATCHES * SEQ, DM),
        "in_w": a[m + "in_proj_w"].T,
        "conv_w": by_partition(a[m + "conv_w"][:, 0, :]),
        "conv_b": by_partition(a[m + "conv_b"]),
        "xproj_w": by_partition(a[m + "x_proj_w"].T),
        "dt_w": a[m + "dt_proj_w"].T,
        "dt_b": by_partition(a[m + "dt_bias"]),
        "a_log": by_partition(a[m + "A_log"]),
        "d_skip": by_partition(a[m + "D_skip"]),
        "out_w": by_partition(a[m + "out_proj_w"].T),
        "router_w": a[f + "router_w"].T,
        "router_b": np.broadcast_to(a[f + "router_bias"], (P, NE)),
        "sw1": a[f + "sw1"], "sw3": a[f + "sw3"], "sw2": by_partition(a[f + "sw2"]),
        "ew1": a[f + "ew1"].swapaxes(0, 1), "ew2": a[f + "ew2"].swapaxes(0, 1),
        "wq": to_rows(a[t + "Wq"]), "bq": to_rows(a[t + "bq"][None]).T,
        "wk": to_rows(a[t + "Wk"]), "bk": to_rows(a[t + "bk"][None], ones_between=True).T,
        "wv": a[t + "Wv"], "bv": a[t + "bv"][None],
        "wo": by_partition(a[t + "Wo"]), "bo": a[t + "bo"][None],
        "fc_w": a[s + "W_fc"].T,
        "proj_w": by_partition(a[s + "W_proj"].T).reshape(P, HF * DM),
        "ln_w": by_partition(a[s + "ln_w"]), "ln_b": by_partition(a[s + "ln_b"]),
        "pick": pick,
    }
    arrays = {k: np.ascontiguousarray(v) for k, v in arrays.items()}
    nc = bacc.Bacc("TRN2", target_bir_lowering=False, num_devices=1)
    d = {k: nc.dram_tensor("in_" + k, v.shape, F32, kind="ExternalInput").ap() for k, v in arrays.items()}
    out = nc.dram_tensor("out", (BATCHES * SEQ, DM), F32, kind="ExternalOutput").ap()
    build(nc, d, out)
    r = run_bass_kernel_spmd(nc, [{"in_" + k: v for k, v in arrays.items()}], core_ids=[0])
    return r.results[0]["out"].reshape(BATCHES, SEQ, DM)
```
